# Optimizing a Trainium2 kernel written in Bass

```python
import numpy as np
import jax
import jax.numpy as jnp

def _softmax(x, axis=-1):
    return jax.nn.softmax(x, axis=axis)

def _gelu(x):
    return jax.nn.gelu(x, approximate=True)

def _silu(x):
    return jax.nn.silu(x)

def _sigmoid(x):
    return jax.nn.sigmoid(x)

def _layernorm(x, axis=-1, eps=1e-05):
    m = jnp.mean(x, axis=axis, keepdims=True)
    v = jnp.var(x, axis=axis, keepdims=True)
    return (x - m) / jnp.sqrt(v + eps)

def _scatter_add(tgt, idx, src, axis=0):
    return tgt.at[idx].add(src)

def _segment_sum(src, seg, n):
    return jax.ops.segment_sum(src, seg, n)
kernel_name = 'mk_dlrm_tower_d1_rec_r8_3e0854'

def setup_inputs(seed: int=0):
    np.random.seed(seed)
    _w = jnp.asarray

    def _rec_inputs():
        import jax
        import jax.numpy as jnp
        _tk = jax.random.key(seed)
        dense_ctx = jax.random.normal(jax.random.fold_in(_tk, 190), (2048, 16), jnp.float32)
        ids = jnp.stack([jax.random.randint(jax.random.fold_in(_tk, 200 + f), (2048,), 0, v, jnp.int32) for f, v in enumerate([1250, 12500, 125000, 1250, 1000, 1250, 12500, 12500, 12500, 1250, 1250, 1250, 1000, 12500, 12500, 1250, 1000, 1250, 12500, 1000, 12500, 1250, 1000, 1250, 1250, 1000, 1250])], axis=1)
        tbl_0 = 0.05 * jax.random.normal(jax.random.fold_in(_tk, 500 + 0), (1250, 128), jnp.float32)
        tbl_1 = 0.05 * jax.random.normal(jax.random.fold_in(_tk, 500 + 1), (12500, 128), jnp.float32)
        tbl_2 = 0.05 * jax.random.normal(jax.random.fold_in(_tk, 500 + 2), (125000, 128), jnp.float32)
        tbl_3 = 0.05 * jax.random.normal(jax.random.fold_in(_tk, 500 + 3), (1250, 128), jnp.float32)
        tbl_4 = 0.05 * jax.random.normal(jax.random.fold_in(_tk, 500 + 4), (1000, 128), jnp.float32)
        tbl_5 = 0.05 * jax.random.normal(jax.random.fold_in(_tk, 500 + 5), (1250, 128), jnp.float32)
        tbl_6 = 0.05 * jax.random.normal(jax.random.fold_in(_tk, 500 + 6), (12500, 128), jnp.float32)
        tbl_7 = 0.05 * jax.random.normal(jax.random.fold_in(_tk, 500 + 7), (12500, 128), jnp.float32)
        tbl_8 = 0.05 * jax.random.normal(jax.random.fold_in(_tk, 500 + 8), (12500, 128), jnp.float32)
        tbl_9 = 0.05 * jax.random.normal(jax.random.fold_in(_tk, 500 + 9), (1250, 128), jnp.float32)
        tbl_10 = 0.05 * jax.random.normal(jax.random.fold_in(_tk, 500 + 10), (1250, 128), jnp.float32)
        tbl_11 = 0.05 * jax.random.normal(jax.random.fold_in(_tk, 500 + 11), (1250, 128), jnp.float32)
        tbl_12 = 0.05 * jax.random.normal(jax.random.fold_in(_tk, 500 + 12), (1000, 128), jnp.float32)
        tbl_13 = 0.05 * jax.random.normal(jax.random.fold_in(_tk, 500 + 13), (12500, 128), jnp.float32)
        tbl_14 = 0.05 * jax.random.normal(jax.random.fold_in(_tk, 500 + 14), (12500, 128), jnp.float32)
        tbl_15 = 0.05 * jax.random.normal(jax.random.fold_in(_tk, 500 + 15), (1250, 128), jnp.float32)
        tbl_16 = 0.05 * jax.random.normal(jax.random.fold_in(_tk, 500 + 16), (1000, 128), jnp.float32)
        tbl_17 = 0.05 * jax.random.normal(jax.random.fold_in(_tk, 500 + 17), (1250, 128), jnp.float32)
        tbl_18 = 0.05 * jax.random.normal(jax.random.fold_in(_tk, 500 + 18), (12500, 128), jnp.float32)
        tbl_19 = 0.05 * jax.random.normal(jax.random.fold_in(_tk, 500 + 19), (1000, 128), jnp.float32)
        tbl_20 = 0.05 * jax.random.normal(jax.random.fold_in(_tk, 500 + 20), (12500, 128), jnp.float32)
        tbl_21 = 0.05 * jax.random.normal(jax.random.fold_in(_tk, 500 + 21), (1250, 128), jnp.float32)
        tbl_22 = 0.05 * jax.random.normal(jax.random.fold_in(_tk, 500 + 22), (1000, 128), jnp.float32)
        tbl_23 = 0.05 * jax.random.normal(jax.random.fold_in(_tk, 500 + 23), (1250, 128), jnp.float32)
        tbl_24 = 0.05 * jax.random.normal(jax.random.fold_in(_tk, 500 + 24), (1250, 128), jnp.float32)
        tbl_25 = 0.05 * jax.random.normal(jax.random.fold_in(_tk, 500 + 25), (1000, 128), jnp.float32)
        tbl_26 = 0.05 * jax.random.normal(jax.random.fold_in(_tk, 500 + 26), (1250, 128), jnp.float32)
        _rk = jax.random.fold_in(_tk, 7)
        W_top1 = 0.0521996 * jax.random.normal(jax.random.fold_in(_tk, 801), (367, 512), jnp.float32)
        W_top2 = 0.0441942 * jax.random.normal(jax.random.fold_in(_tk, 802), (512, 256), jnp.float32)
        W_top3 = 0.0625 * jax.random.normal(jax.random.fold_in(_tk, 803), (256, 1), jnp.float32)
        b_top1 = jnp.zeros((512,), jnp.float32)
        b_top2 = jnp.zeros((256,), jnp.float32)
        return (dense_ctx, ids, tbl_0, tbl_1, tbl_2, tbl_3, tbl_4, tbl_5, tbl_6, tbl_7, tbl_8, tbl_9, tbl_10, tbl_11, tbl_12, tbl_13, tbl_14, tbl_15, tbl_16, tbl_17, tbl_18, tbl_19, tbl_20, tbl_21, tbl_22, tbl_23, tbl_24, tbl_25, tbl_26, W_top1, b_top1, W_top2, b_top2, W_top3)
    dense_ctx, ids, tbl_0, tbl_1, tbl_2, tbl_3, tbl_4, tbl_5, tbl_6, tbl_7, tbl_8, tbl_9, tbl_10, tbl_11, tbl_12, tbl_13, tbl_14, tbl_15, tbl_16, tbl_17, tbl_18, tbl_19, tbl_20, tbl_21, tbl_22, tbl_23, tbl_24, tbl_25, tbl_26, W_top1, b_top1, W_top2, b_top2, W_top3 = _rec_inputs()

    def _L0_rec_setup():
        import jax, jax.numpy as jnp
        import numpy as np
        NUM_FEATURES = 27
        EMBED_DIM = 128
        BATCH = 4096
        key = jax.random.key(seed)
        inputs = jax.random.normal(key, (BATCH, NUM_FEATURES, EMBED_DIM), dtype=jnp.float32)
        return {'inputs': inputs}
    _L0_rec_all = _L0_rec_setup()
    _L0_rec_in = {k: v for k, v in _L0_rec_all.items() if k in ()}
    del _L0_rec_all
    return {'dense_ctx': dense_ctx, 'ids': ids, 'tbl_0': tbl_0, 'tbl_1': tbl_1, 'tbl_2': tbl_2, 'tbl_3': tbl_3, 'tbl_4': tbl_4, 'tbl_5': tbl_5, 'tbl_6': tbl_6, 'tbl_7': tbl_7, 'tbl_8': tbl_8, 'tbl_9': tbl_9, 'tbl_10': tbl_10, 'tbl_11': tbl_11, 'tbl_12': tbl_12, 'tbl_13': tbl_13, 'tbl_14': tbl_14, 'tbl_15': tbl_15, 'tbl_16': tbl_16, 'tbl_17': tbl_17, 'tbl_18': tbl_18, 'tbl_19': tbl_19, 'tbl_20': tbl_20, 'tbl_21': tbl_21, 'tbl_22': tbl_22, 'tbl_23': tbl_23, 'tbl_24': tbl_24, 'tbl_25': tbl_25, 'tbl_26': tbl_26, 'W_top1': W_top1, 'b_top1': b_top1, 'W_top2': W_top2, 'b_top2': b_top2, 'W_top3': W_top3}

def reference(dense_ctx, ids, tbl_0, tbl_1, tbl_2, tbl_3, tbl_4, tbl_5, tbl_6, tbl_7, tbl_8, tbl_9, tbl_10, tbl_11, tbl_12, tbl_13, tbl_14, tbl_15, tbl_16, tbl_17, tbl_18, tbl_19, tbl_20, tbl_21, tbl_22, tbl_23, tbl_24, tbl_25, tbl_26, W_top1, b_top1, W_top2, b_top2, W_top3):
    import jax
    import jax.numpy as jnp

    def _L0_rec_ref(inputs):
        import jax, jax.numpy as jnp
        import numpy as np
        NUM_FEATURES = 27
        EMBED_DIM = 128
        BATCH = 4096
        interactions = jnp.einsum('bnd,bmd->bnm', inputs, inputs)
        n = inputs.shape[1]
        i, j = jnp.triu_indices(n, k=1)
        return interactions[:, i, j]
    e = jnp.stack([tbl_0[ids[:, 0]], tbl_1[ids[:, 1]], tbl_2[ids[:, 2]], tbl_3[ids[:, 3]], tbl_4[ids[:, 4]], tbl_5[ids[:, 5]], tbl_6[ids[:, 6]], tbl_7[ids[:, 7]], tbl_8[ids[:, 8]], tbl_9[ids[:, 9]], tbl_10[ids[:, 10]], tbl_11[ids[:, 11]], tbl_12[ids[:, 12]], tbl_13[ids[:, 13]], tbl_14[ids[:, 14]], tbl_15[ids[:, 15]], tbl_16[ids[:, 16]], tbl_17[ids[:, 17]], tbl_18[ids[:, 18]], tbl_19[ids[:, 19]], tbl_20[ids[:, 20]], tbl_21[ids[:, 21]], tbl_22[ids[:, 22]], tbl_23[ids[:, 23]], tbl_24[ids[:, 24]], tbl_25[ids[:, 25]], tbl_26[ids[:, 26]]], axis=1)
    z = _L0_rec_ref(e)
    z = z.reshape(z.shape[0], -1)
    h = jnp.concatenate([z, dense_ctx], axis=1)
    h = jnp.maximum(h @ W_top1 + b_top1, 0.0)
    h = jnp.maximum(h @ W_top2 + b_top2, 0.0)
    y = h @ W_top3
    return y

_drawn_inputs = setup_inputs


def setup_inputs(seed=0):
    import zlib

    import numpy as np

    out = dict(_drawn_inputs(seed))
    spreads = {'b_top1': (0.0, 0.1), 'b_top2': (0.0, 0.1)}
    factors = {}
    for name, (base, spread) in spreads.items():
        noise = np.random.default_rng([zlib.crc32(name.encode()), seed]).standard_normal(out[name].shape)
        drawn = base * np.exp(spread * noise) if base else spread * noise
        out[name] = jnp.asarray(drawn.astype(out[name].dtype))
    for name, factor in factors.items():
        out[name] = (out[name] * factor).astype(out[name].dtype)
    return out
```

```python
from contextlib import ExitStack

import concourse.bass as bass
from concourse import mybir

ALU = mybir.AluOpType
ACT = mybir.ActivationFunctionType
F32 = mybir.dt.float32
I32 = mybir.dt.int32

P = 128
DMA = 16


def dlrm_tower(nc, dense_ctx, ids, tables, W1, b1, W2, b2, W3, out):
    batch, F = ids.shape
    D = tables[0].shape[1]
    ND = dense_ctx.shape[1]
    H1, H2 = W1.shape[1], W2.shape[1]
    TILES = batch // P
    UT = 2
    UNITS = TILES // UT
    UB = UT * P
    GROUP = 4
    QP = P // GROUP
    PAIRS = F * (F - 1) // 2
    K1 = -(-(PAIRS + ND) // P)
    C1, C2 = H1 // P, H2 // P
    BANK = 512
    assert D == P and F <= QP and PAIRS + ND == W1.shape[0] and TILES % UT == 0

    TG = [(f, min(f + 4, F)) for f in range(0, F, 4)]
    NT = len(TG)
    T_DVE, T_ACT = (NT + 1) // 2, NT // 2
    SG = 8
    NS = P // GROUP // SG

    segments = []
    row = 0
    for i in range(F - 1):
        j = i + 1
        while j < F:
            n = min(F - j, P - row % P)
            segments.append((i, j, n, row // P, row % P))
            row, j = row + n, j + n
    dense_row = (row // P, row % P)
    assert row == PAIRS and row % P + ND <= P
    ZD = DMA * (len(segments) + 1)
    M_STEPS = C1 + C2 + 1

    with ExitStack() as ctx:
        def sb(name, shape, dt=F32):
            return ctx.enter_context(nc.sbuf_tensor(name, shape, dt))

        def sem(name):
            return ctx.enter_context(nc.semaphore(name))

        ids_sb = sb("ids_sb", [P, TILES, F], I32)
        idx = sb("idx", [P, UT, F], I32)
        dense_sb = sb("dense_sb", [P, TILES, ND])
        denseT = sb("denseT", [ND, TILES, P])
        W1_sb = sb("W1_sb", [P, K1, H1])
        W2_sb = sb("W2_sb", [P, C1, H2])
        W3_sb = sb("W3_sb", [P, C2])
        b1_sb = sb("b1_sb", [P, C1])
        b2_sb = sb("b2_sb", [P, C2])
        ident = sb("ident", [P, P])
        E = [sb(f"E{u}", [P, F, D]) for u in range(UT)]
        ET = [sb(f"ET{u}", [P, P, QP]) for u in range(UT)]
        Gs = [sb(f"Gs{u}", [F, F, P]) for u in range(UT)]
        Z = sb("Z", [P, K1, UB])
        h1 = sb("h1", [P, C1, UB])
        h2 = sb("h2", [P, C2, UB])
        y_sb = sb("y_sb", [1, P, TILES])

        psT = [ctx.enter_context(nc.psum_tensor(f"psT{n}", [P, 4, P], F32)) for n in range(2)]
        psG = [ctx.enter_context(nc.psum_tensor(f"psG{n}", [P, 2, BANK], F32)) for n in range(2)]
        psM = [ctx.enter_context(nc.psum_tensor(f"psM{n}", [P, BANK], F32)) for n in range(2)]

        ids_landed = sem("ids_landed")
        dense_landed = sem("dense_landed")
        weights_landed = sem("weights_landed")
        cleared = sem("cleared")
        ident_ready = sem("ident_ready")
        idx_ready = sem("idx_ready")
        gathered = [[sem(f"gathered{u}_{q}") for q in range(NT)] for u in range(UT)]
        slot_free = sem("slot_free")
        dense_t_done = sem("dense_t_done")
        dense_ready = sem("dense_ready")
        t_done = sem("t_done")
        et_dve = sem("et_dve")
        et_act = sem("et_act")
        g_done = sem("g_done")
        gs_dve = sem("gs_dve")
        gs_act = sem("gs_act")
        z_landed = [sem(f"z_landed{u}") for u in range(UT)]
        m_done = sem("m_done")
        relu_done = sem("relu_done")
        y_ready = sem("y_ready")
        out_landed = sem("out_landed")

        block = ctx.enter_context(nc.Block())

        dense_banks = [psT[0], psT[1], psM[0], psM[1]]
        DG = TILES // 4

        @block.sync
        def _(sp):
            sp.dma_start(ids_sb[:], ids.rearrange("(p t) f -> p t f", t=TILES)).then_inc(ids_landed, DMA)
            sp.dma_start(dense_sb[:], dense_ctx.rearrange("(p t) f -> p t f", t=TILES)).then_inc(dense_landed, DMA)
            for c in range(K1):
                n = min(P, W1.shape[0] - c * P)
                sp.dma_start(W1_sb[0:n, c, :], W1[c * P:c * P + n, :]).then_inc(weights_landed, DMA)
            sp.dma_start(W2_sb[:], W2.rearrange("(c p) n -> p c n", p=P)).then_inc(weights_landed, DMA)
            with nc.allow_non_contiguous_dma("vectors, once"):
                sp.dma_start(W3_sb[:], W3.rearrange("(c p) n -> p (c n)", p=P)).then_inc(weights_landed, DMA)
                sp.dma_start(b1_sb[:], b1.rearrange("(c p) -> p c", p=P)).then_inc(weights_landed, DMA)
                sp.dma_start(b2_sb[:], b2.rearrange("(c p) -> p c", p=P)).then_inc(weights_landed, DMA)
            sp.wait_ge(dense_ready, DG)

            def scatter_tile(i, u, first):
                t = UT * i + u
                sp.wait_ge(gs_dve, NS * t + NS)
                sp.wait_ge(gs_act, NS * t + NS)
                if not first:
                    sp.wait_ge(m_done, M_STEPS * (i - 1) + C1)
                for fi, j, n, c, r in segments:
                    sp.dma_start(Z[r:r + n, c, u * P:(u + 1) * P], Gs[u][fi:fi + 1, j:j + n, :])\
                      .then_inc(z_landed[u], DMA)
                c, r = dense_row
                sp.dma_start(Z[r:r + ND, c, u * P:(u + 1) * P], denseT[:, bass.ts(t, 1), :])\
                  .then_inc(z_landed[u], DMA)

            for u in range(UT):
                scatter_tile(0, u, True)
            with sp.Fori(1, UNITS) as i:
                for u in range(UT):
                    scatter_tile(i, u, False)
            sp.wait_ge(y_ready, UNITS)
            sp.dma_start(out.rearrange("b o -> o b"), y_sb[:, :, :].rearrange("o p t -> o (p t)"))\
              .then_inc(out_landed, DMA)
            sp.wait_ge(out_landed, DMA)

        @block.gpsimd
        def _(pool):
            pool.memset(ident[:], 0.0).then_inc(cleared, 1)
            for u in range(UT):
                pool.memset(ET[u][:, :, F:], 0.0).then_inc(cleared, 1)
            pool.wait_ge(cleared, 1 + UT)
            pool.affine_select(out=ident[:], in_=ident[:], compare_op=ALU.not_equal, fill=1.0, base=0,
                               pattern=[[-1, P]], channel_multiplier=1).then_inc(ident_ready, 1)

            def gather_tile(i, u, first):
                t = UT * i + u
                pool.wait_ge(idx_ready, t + 1)
                pool.sem_inc(slot_free, 1)
                for q, (f0, f1) in enumerate(TG):
                    if not first:
                        pool.wait_ge(t_done, NT * (t - UT) + q + 1)
                        pool.sem_inc(slot_free, 1)
                    for f in range(f0, f1):
                        pool.indirect_dma_start(
                            E[u][:, f, :], None, tables[f],
                            bass.IndirectOffsetOnAxis(ap=idx[:, u, f:f + 1], axis=0),
                        ).then_inc(gathered[u][q], DMA)

            for u in range(UT):
                gather_tile(0, u, True)
            with pool.Fori(1, UNITS) as i:
                for u in range(UT):
                    gather_tile(i, u, False)

        @block.tensor
        def _(pe):
            pe.wait_ge(ident_ready, 1)
            pe.wait_ge(dense_landed, DMA)
            for g in range(DG):
                for k in range(4):
                    last = pe.transpose(dense_banks[g][0:ND, k * P:(k + 1) * P] if g >= 2 else
                                        dense_banks[g][0:ND, k, :], dense_sb[:, 4 * g + k, :], ident[:])
                last.then_inc(dense_t_done, 1)

            def transposes(i, u):
                t = UT * i + u
                for q, (f0, f1) in enumerate(TG):
                    pe.wait_ge(gathered[u][q], DMA * (f1 - f0) * (i + 1))
                    if q >= 2:
                        if q % 2:
                            pe.wait_ge(et_act, T_ACT * t + (q - 1) // 2)
                        else:
                            pe.wait_ge(et_dve, T_DVE * t + q // 2)
                    elif not (isinstance(t, int) and t == 0):
                        pe.wait_ge(et_dve if q else et_act, (T_DVE if q else T_ACT) * t)
                    else:
                        pe.wait_ge(dense_ready, DG)
                    for f in range(f0, f1):
                        last = pe.transpose(psT[(u + q) % 2][:, f - f0, :], E[u][:, f, :], ident[:])
                    last.then_inc(t_done, 1)

            def dot_products(i, u, first):
                t = UT * i + u
                pe.wait_ge(et_dve, T_DVE * t + T_DVE)
                pe.wait_ge(et_act, T_ACT * t + T_ACT)
                for s in range(NS):
                    if not (first and s < 2):
                        pe.wait_ge(gs_dve, NS * t + s - 1)
                        pe.wait_ge(gs_act, NS * t + s - 1)
                    for m in range(SG):
                        b = GROUP * (s * SG + m)
                        stationary = ET[u][:, b:b + GROUP, :].rearrange("d b f -> d (b f)")
                        moving = ET[u][:, b:b + GROUP, 0:F]
                        half = SG // 2
                        last = pe.matmul(psG[s % 2][:, m // half, (m % half) * GROUP * F:(m % half + 1) * GROUP * F],
                                         stationary, moving, start=True, stop=True)
                    last.then_inc(g_done, 1)

            def mlp(i, first):
                for u in range(UT):
                    pe.wait_ge(z_landed[u], ZD * i + ZD)
                if first:
                    pe.wait_ge(weights_landed, DMA * (K1 + 4))
                for m in range(C1):
                    if m == 0:
                        if not first:
                            pe.wait_ge(y_ready, i)
                            pe.wait_ge(relu_done, (C1 + C2) * i)
                    elif m >= 2:
                        pe.wait_ge(relu_done, (C1 + C2) * i + m - 1)
                    for c in range(K1):
                        n = min(P, W1.shape[0] - c * P)
                        last = pe.matmul(psM[m % 2][:, 0:UB], W1_sb[0:n, c, m * P:(m + 1) * P], Z[0:n, c, :],
                                         start=(c == 0), stop=(c == K1 - 1))
                    last.then_inc(m_done, 1)
                pe.wait_ge(relu_done, (C1 + C2) * i + C1)
                for m in range(C2):
                    for c in range(C1):
                        last = pe.matmul(psM[(C1 + m) % 2][:, 0:UB], W2_sb[:, c, m * P:(m + 1) * P], h1[:, c, :],
                                         start=(c == 0), stop=(c == C1 - 1))
                    last.then_inc(m_done, 1)
                pe.wait_ge(relu_done, (C1 + C2) * i + C1 + C2)
                for c in range(C2):
                    last = pe.matmul(psM[0][0:1, 0:UB], W3_sb[:, c:c + 1], h2[:, c, :],
                                     start=(c == 0), stop=(c == C2 - 1))
                last.then_inc(m_done, 1)

            transposes(0, 0)
            transposes(0, 1)
            dot_products(0, 0, True)
            with pe.Fori(1, UNITS) as i:
                transposes(i, 0)
                dot_products(i - 1, 1, False)
                transposes(i, 1)
                dot_products(i, 0, False)
                mlp_unit = i - 1
                mlp(mlp_unit, False)
            dot_products(UNITS - 1, 1, False)
            mlp(UNITS - 1, False)

        def copy_et(eng, copy, i, u, q, first, done):
            t = UT * i + u
            f0, f1 = TG[q]
            eng.wait_ge(t_done, NT * t + q + 1)
            if not first:
                eng.wait_ge(g_done, NS * (t - UT) + NS)
            dst = ET[u][:, :, f0:f1].rearrange("d p f -> d f p")
            copy(dst, psT[(u + q) % 2][:, 0:f1 - f0, :]).then_inc(done, 1)

        def copy_gs(eng, copy, i, u, quarters, first, done):
            t = UT * i + u
            if not first:
                eng.wait_ge(z_landed[u], ZD * i)
            for s in range(NS):
                eng.wait_ge(g_done, NS * t + s + 1)
                for g in quarters:
                    src = psG[s % 2][QP * g:QP * g + F, :, 0:SG // 2 * GROUP * F]\
                        .rearrange("i h (n c) -> i h n c", c=GROUP * F)[:, :, :, g * F:(g + 1) * F]
                    dst = Gs[u][:, :, s * SG * GROUP:(s + 1) * SG * GROUP]\
                        .rearrange("i j (h n c) -> i h n j c", h=2, c=GROUP)[:, :, :, :, g]
                    last = copy(dst, src)
                last.then_inc(done, 1)

        @block.vector
        def _(dve):
            dve.wait_ge(ids_landed, DMA)
            for u in range(UT):
                dve.tensor_copy(idx[:, u, :], ids_sb[:, u, :]).then_inc(idx_ready, 1)
            for g in range(2):
                dve.wait_ge(dense_t_done, g + 1)
                dve.tensor_copy(denseT[:, 4 * g:4 * g + 4, :], psT[g][0:ND, :, :]).then_inc(dense_ready, 1)
            dve.wait_ge(cleared, 1 + UT)

            def tile_in(i, u, first):
                for q in range(0, NT, 2):
                    copy_et(dve, dve.tensor_copy, i, u, q, first, et_dve)

            def next_indices(i, u):
                dve.tensor_copy(idx[:, u:u + 1, :], ids_sb[:, bass.ts(UT * (i + 1) + u, 1), :]).then_inc(idx_ready, 1)

            def write_y(i, first):
                dve.wait_ge(m_done, M_STEPS * i + M_STEPS)
                dve.tensor_copy(y_sb[:, :, bass.ds(UT * i, UT)].rearrange("o p t -> o t p"),
                                psM[0][0:1, 0:UB].rearrange("o (t p) -> o t p", t=UT)).then_inc(y_ready, 1)

            tile_in(0, 0, True)
            next_indices(0, 0)
            tile_in(0, 1, True)
            next_indices(0, 1)
            copy_gs(dve, dve.tensor_copy, 0, 0, (0, 1), True, gs_dve)
            with dve.Fori(1, UNITS - 1) as i:
                tile_in(i, 0, False)
                next_indices(i, 0)
                copy_gs(dve, dve.tensor_copy, i - 1, 1, (0, 1), False, gs_dve)
                tile_in(i, 1, False)
                next_indices(i, 1)
                copy_gs(dve, dve.tensor_copy, i, 0, (0, 1), False, gs_dve)
                write_y(i - 1, False)
            i = UNITS - 1
            tile_in(i, 0, False)
            copy_gs(dve, dve.tensor_copy, i - 1, 1, (0, 1), False, gs_dve)
            tile_in(i, 1, False)
            copy_gs(dve, dve.tensor_copy, i, 0, (0, 1), False, gs_dve)
            write_y(i - 1, False)
            copy_gs(dve, dve.tensor_copy, i, 1, (0, 1), False, gs_dve)
            write_y(i, False)

        @block.scalar
        def _(act):
            for g in range(2, DG):
                act.wait_ge(dense_t_done, g + 1)
                act.copy(denseT[:, 4 * g:4 * g + 4, :],
                         dense_banks[g][0:ND, :].rearrange("d (t p) -> d t p", t=4)).then_inc(dense_ready, 1)
            act.wait_ge(weights_landed, DMA * (K1 + 4))

            def tile_in(i, u, first):
                for q in range(1, NT, 2):
                    copy_et(act, act.copy, i, u, q, first, et_act)

            def relus(i):
                for m in range(C1):
                    act.wait_ge(m_done, M_STEPS * i + m + 1)
                    act.activation(h1[:, m, :], psM[m % 2][:, 0:UB], ACT.Relu, bias=b1_sb[:, m:m + 1])\
                       .then_inc(relu_done, 1)
                for m in range(C2):
                    act.wait_ge(m_done, M_STEPS * i + C1 + m + 1)
                    act.activation(h2[:, m, :], psM[(C1 + m) % 2][:, 0:UB], ACT.Relu, bias=b2_sb[:, m:m + 1])\
                       .then_inc(relu_done, 1)

            tile_in(0, 0, True)
            tile_in(0, 1, True)
            copy_gs(act, act.copy, 0, 0, (2, 3), True, gs_act)
            with act.Fori(1, UNITS) as i:
                tile_in(i, 0, False)
                copy_gs(act, act.copy, i - 1, 1, (2, 3), False, gs_act)
                tile_in(i, 1, False)
                copy_gs(act, act.copy, i, 0, (2, 3), False, gs_act)
                relus(i - 1)
            copy_gs(act, act.copy, UNITS - 1, 1, (2, 3), False, gs_act)
            relus(UNITS - 1)


def kernel(**inputs):
    import numpy as np
    import concourse.bacc as bacc
    from concourse.bass_utils import run_bass_kernel_spmd

    nc = bacc.Bacc("TRN2", target_bir_lowering=False, num_devices=1)
    arrays, aps = {}, {}
    for name, value in inputs.items():
        arrays[f"in_{name}"] = np.ascontiguousarray(value)
        a = arrays[f"in_{name}"]
        aps[name] = nc.dram_tensor(f"in_{name}", a.shape, mybir.dt.from_np(a.dtype), kind="ExternalInput").ap()
    batch, features = inputs["ids"].shape
    out = nc.dram_tensor("y_out", (batch, 1), F32, kind="ExternalOutput").ap()
    dlrm_tower(nc, aps["dense_ctx"], aps["ids"], [aps[f"tbl_{f}"] for f in range(features)],
               aps["W_top1"], aps["b_top1"], aps["W_top2"], aps["b_top2"], aps["W_top3"], out)
    result = run_bass_kernel_spmd(nc, [arrays], core_ids=[0])
    return result.results[0]["y_out"]
```

```python
from contextlib import ExitStack

import concourse.bass as bass
from concourse import mybir

ALU = mybir.AluOpType
ACT = mybir.ActivationFunctionType
F32 = mybir.dt.float32
F32R = mybir.dt.float32r
I32 = mybir.dt.int32

P = 128
DMA = 16
SPLIT_ROWS = 125
ONEHOT = (4, 12, 16, 19, 22, 24, 25, 26)
GATHERED = ((0, 1, 4), (5, 1, 4), (9, 1, 3), (13, 1, 3), (17, 3, 3), (18, 3, 2))


def spread(few, many):
    steps, taken = [], 0
    for n, step in enumerate(few):
        steps.append(step)
        upto = len(many) * (n + 1) // len(few)
        steps += many[taken:upto]
        taken = upto
    return steps


def weight_order(F, rows):
    pair = {}
    for i in range(F):
        for j in range(i + 1, F):
            pair[i, j] = len(pair)
    order = [pair[min(i, (i + s) % F), max(i, (i + s) % F)]
             for s in range(F // 2, 0, -1) for i in range(F - 1, -1, -1)]
    return order + list(range(len(pair), rows))


def dlrm_tower(nc, dense_ctx, ids, tables, W1, b1, W2, b2, W3, out):
    batch, F = ids.shape
    D = tables[0].shape[1]
    ND = dense_ctx.shape[1]
    H1, H2 = W1.shape[1], W2.shape[1]
    TILES = batch // P
    UT = 2
    UNITS = TILES // UT
    UB = UT * P
    GROUP = 4
    QP = P // GROUP
    PAIRS = F * (F - 1) // 2
    K1 = -(-(PAIRS + ND) // P)
    C1, C2 = H1 // P, H2 // P
    assert D == P and F <= QP and PAIRS + ND == W1.shape[0] and TILES % UT == 0

    TG = [[f0 + step * n for n in range(count)] for f0, step, count in GATHERED]
    NT = len(TG)
    TH = NT // 2
    assert NT % 2 == 0 and sorted(sum(TG, []) + list(ONEHOT)) == list(range(F))
    slot_of = {f: n for n, f in enumerate(sum(TG, []))}
    NF = len(slot_of)

    NO = len(ONEHOT)
    VR = SPLIT_ROWS
    chunks = [tables[f].shape[0] // VR for f in ONEHOT]
    first_chunk = [sum(chunks[:n]) for n in range(NO)]
    CMAX = max(chunks)
    kinds = sorted(set(chunks))
    RP = NO // 2
    assert all(tables[f].shape[0] % VR == 0 for f in ONEHOT) and NO % 4 == 0

    SG = 4
    NS = P // GROUP // SG
    VQ, AQ = (0,), (1, 2, 3)

    S = F // 2
    assert F % 2 and S * F == PAIRS
    BLOCKS = ((0, S + 1, 1, F, 0), (S + 1, F, S + 2, F, 0), (S + 1, F, 0, S, 1))
    DRAM_ROWS = F * (S + 2 * F)
    Z_START = F * F - S * F - (F - 1)
    z_parts = [(c, min(P, PAIRS - c * P)) for c in range(K1)]
    dense_row = PAIRS - (K1 - 1) * P
    assert 0 < dense_row and dense_row + ND <= P
    ZD = DMA * (K1 + 1)
    MS = C1 + C2 + 1
    RELUS = C1 + C2
    WEIGHT_DMAS = K1 + 4

    g_steps = [("G", s) for s in range(NS)]
    o_steps = [("O", k) for k in range(NO)]
    t_steps = [("T", q) for q in range(NT)]
    m_steps = [("M", m) for m in range(MS)]
    PHASE_A = spread(t_steps, g_steps + o_steps)
    PHASE_B = spread(t_steps, [g_steps[0]] + [step for n in range(MS) for step in (m_steps[n], g_steps[n + 1])])
    assert MS + 1 == NS

    with ExitStack() as ctx:
        def sb(name, shape, dt=F32):
            return ctx.enter_context(nc.sbuf_tensor(name, shape, dt))

        def bank(name):
            return ctx.enter_context(nc.psum_tensor(name, [P, 4, P], F32))

        def sem(name):
            return ctx.enter_context(nc.semaphore(name))

        ids_sb = sb("ids_sb", [P, TILES, F], I32)
        idx = sb("idx", [P, UT, F], I32)
        rows = sb("rows", [P, TILES, QP + ND])
        idsT = sb("idsT", [F, TILES, P], F32R)
        wide = sb("wide", [P, TILES * P])
        denseT = wide[0:ND, :].rearrange("d (t p) -> d t p", t=TILES)
        y_sb = wide[QP:QP + 1, :].rearrange("o (p t) -> o p t", t=TILES)
        W1_sb = sb("W1_sb", [P, K1, H1])
        W2_sb = sb("W2_sb", [P, C1, H2])
        W3_sb = sb("W3_sb", [P, C2])
        b1_sb = sb("b1_sb", [P, C1])
        b2_sb = sb("b2_sb", [P, C2])
        ident = sb("ident", [P, P])
        select = sb("select", [F, NO, VR], F32R)
        number = [sb(f"number{c}", [VR, c], I32) for c in kinds]
        numberf = [sb(f"numberf{c}", [VR, c]) for c in kinds]
        high = sb("high", [VR, sum(chunks), D], F32R)
        low = sb("low", [VR, sum(chunks), D], F32R)
        index = sb("index", [VR, 2, 2, UB])
        onehot = [sb(f"onehot{n}", [VR, CMAX, UB], F32R) for n in range(2)]
        E = [sb(f"E{u}", [P, NF, D]) for u in range(UT)]
        ET = sb("ET", [P, UT, P, QP])
        Gs_all = sb("Gs_all", [P, F, P])
        Gs = [Gs_all[P // UT * u:P // UT * u + F, :, :] for u in range(UT)]
        raw = [Gs_all[0:VR, n * F // 2:n * F // 2 + CMAX, :] for n in range(2)]
        spread_rows = [nc.dram_tensor(f"spread_rows{u}", [DRAM_ROWS, P], F32, kind="Internal").ap() for u in range(UT)]
        Z = sb("Z", [P, K1, UB])
        h1 = sb("h1", [P, C1, UB])
        h2 = sb("h2", [P, C2, UB])

        psT = [bank(f"psT{n}") for n in range(2)]
        psG = [bank(f"psG{n}") for n in range(2)]
        psM = bank("psM")
        psR = bank("psR")
        psO = [bank(f"psO{n}") for n in range(2)]

        def flat(b):
            return b[:, :, :].rearrange("p a b -> p (a b)")

        def half(b, n):
            return flat(b)[:, n * UB:(n + 1) * UB]

        ids_landed = sem("ids_landed")
        dense_landed = sem("dense_landed")
        weights_landed = sem("weights_landed")
        cleared = sem("cleared")
        ident_ready = sem("ident_ready")
        numbers_made = sem("numbers_made")
        rows_ready = sem("rows_ready")
        select_ready = sem("select_ready")
        raw_landed = [sem(f"raw_landed{n}") for n in range(2)]
        high_ready = sem("high_ready")
        low_ready = sem("low_ready")
        idx_ready = sem("idx_ready")
        gathered = [[sem(f"gathered{u}_{q}") for q in range(NT)] for u in range(UT)]
        slot_free = sem("slot_free")
        rows_t_done = sem("rows_t_done")
        rows_t_dve = sem("rows_t_dve")
        rows_t_act = sem("rows_t_act")
        t_done = sem("t_done")
        et_dve = sem("et_dve")
        et_act = sem("et_act")
        r_done = sem("r_done")
        index_ready = sem("index_ready")
        onehot_ready = sem("onehot_ready")
        o_done = sem("o_done")
        o_copied = sem("o_copied")
        g_done = sem("g_done")
        gs_dve = sem("gs_dve")
        gs_act = sem("gs_act")
        rows_landed = [sem(f"rows_landed{u}") for u in range(UT)]
        z_landed = [sem(f"z_landed{u}") for u in range(UT)]
        m_done = sem("m_done")
        relu_done = sem("relu_done")
        y_ready = sem("y_ready")
        out_landed = sem("out_landed")

        block = ctx.enter_context(nc.Block())

        def wait_since(eng, semaphore, count):
            if not (isinstance(count, int) and count <= 0):
                eng.wait_ge(semaphore, count)

        row_banks = [psT[0], psT[1], psG[0], psG[1]]
        RG = TILES // 4
        assert RG == len(row_banks)

        def weight_rows(c):
            return min(P, W1.shape[0] - c * P)

        @block.sync
        def _(sp):
            sp.dma_start(ids_sb[:], ids.rearrange("(p t) f -> p t f", t=TILES)).then_inc(ids_landed, DMA)

            def load_table(k):
                c = chunks[k]
                sp.dma_start(raw[k % 2][:, 0:c, :], tables[ONEHOT[k]].rearrange("(p c) d -> p c d", c=c))\
                  .then_inc(raw_landed[k % 2], DMA)

            load_table(0)
            sp.dma_start(rows[:, :, QP:], dense_ctx.rearrange("(p t) f -> p t f", t=TILES)).then_inc(dense_landed, DMA)
            load_table(1)
            for k in range(2, NO):
                sp.wait_ge(low_ready, k - 1)
                load_table(k)
            for c in range(K1):
                n = weight_rows(c)
                sp.dma_start(W1_sb[0:n, c, :], W1[c * P:c * P + n, :]).then_inc(weights_landed, DMA)
            sp.dma_start(W2_sb[:], W2.rearrange("(c p) n -> p c n", p=P)).then_inc(weights_landed, DMA)
            with nc.allow_non_contiguous_dma("vectors, once"):
                sp.dma_start(W3_sb[:], W3.rearrange("(c p) n -> p (c n)", p=P)).then_inc(weights_landed, DMA)
                sp.dma_start(b1_sb[:], b1.rearrange("(c p) -> p c", p=P)).then_inc(weights_landed, DMA)
                sp.dma_start(b2_sb[:], b2.rearrange("(c p) -> p c", p=P)).then_inc(weights_landed, DMA)
            sp.wait_ge(rows_t_act, RG)

            def scatter_tile(i, u, first):
                t = UT * i + u
                sp.wait_ge(gs_dve, NS * t + NS)
                sp.wait_ge(gs_act, NS * t + NS)
                for i0, i1, j0, j1, wrap in BLOCKS:
                    scratch = spread_rows[u]
                    start = F * F - (j1 - 1 - i0 + wrap * F) * F - i0
                    dst = bass.AP(tensor=scratch.tensor, offset=scratch.offset + start * P,
                                  ap=[[(F - 1) * P, i1 - i0], [F * P, j1 - j0], [1, P]])
                    sp.dma_start(dst, Gs[u][i0:i1, F - j1:F - j0, :]).then_inc(rows_landed[u], DMA)
                if not first:
                    sp.wait_ge(m_done, MS * (i - 1) + C1)
                sp.dma_start(Z[dense_row:dense_row + ND, K1 - 1, u * P:(u + 1) * P], denseT[:, bass.ts(t, 1), :])\
                  .then_inc(z_landed[u], DMA)
                sp.wait_ge(rows_landed[u], DMA * len(BLOCKS) * (i + 1))
                for c, n in z_parts:
                    start = Z_START + c * P
                    sp.dma_start(Z[0:n, c, u * P:(u + 1) * P], spread_rows[u][start:start + n, :])\
                      .then_inc(z_landed[u], DMA)

            for u in range(UT):
                scatter_tile(0, u, True)
            with sp.Fori(1, UNITS) as i:
                for u in range(UT):
                    scatter_tile(i, u, False)
            sp.wait_ge(y_ready, UNITS)
            sp.dma_start(out.rearrange("b o -> o b"), y_sb.rearrange("o p t -> o (p t)")).then_inc(out_landed, DMA)
            sp.wait_ge(out_landed, DMA)

        @block.gpsimd
        def _(pool):
            def gather_tile(i, u, first):
                t = UT * i + u
                pool.wait_ge(idx_ready, t + 1)
                pool.sem_inc(slot_free, 1)
                for q, group in enumerate(TG):
                    if not first:
                        pool.wait_ge(t_done, NT * (t - UT) + q + 1)
                        pool.sem_inc(slot_free, 1)
                    for f in group:
                        pool.indirect_dma_start(
                            E[u][:, slot_of[f], :], None, tables[f],
                            bass.IndirectOffsetOnAxis(ap=idx[:, u, f:f + 1], axis=0),
                        ).then_inc(gathered[u][q], DMA)

            pool.memset(ident[:], 0.0).then_inc(cleared, 1)
            pool.wait_ge(cleared, 1)
            pool.affine_select(out=ident[:], in_=ident[:], compare_op=ALU.not_equal, fill=1.0, base=0,
                               pattern=[[-1, P]], channel_multiplier=1).then_inc(ident_ready, 1)
            for n, c in enumerate(kinds):
                pool.iota(number[n][:], pattern=[[1, c]], base=0, channel_multiplier=c).then_inc(numbers_made, 1)
            for u in range(UT):
                gather_tile(0, u, True)
            with pool.Fori(1, UNITS) as i:
                for u in range(UT):
                    gather_tile(i, u, False)

        @block.tensor
        def _(pe):
            pe.wait_ge(ident_ready, 1)
            pe.wait_ge(rows_ready, 1)
            pe.wait_ge(dense_landed, DMA)
            for g in range(RG):
                for n in range(4):
                    last = pe.transpose(row_banks[g][0:QP + ND, n, :], rows[:, 4 * g + n, :], ident[:])
                last.then_inc(rows_t_done, 1)

            def T(i, u, q, first):
                t = UT * i + u
                pe.wait_ge(gathered[u][q], DMA * len(TG[q]) * (i + 1))
                if q >= 2 or not first:
                    pe.wait_ge(et_act if q % 2 else et_dve, TH * t + q // 2)
                else:
                    pe.wait_ge(rows_t_dve, RG)
                    pe.wait_ge(rows_t_act, RG)
                for n, f in enumerate(TG[q]):
                    last = pe.transpose(psT[q % 2][:, n, :], E[u][:, slot_of[f], :], ident[:])
                last.then_inc(t_done, 1)

            def R(i, r):
                for n in range(2):
                    last = pe.matmul(half(psR, n)[0:VR, :], select[:, 2 * r + n, :], idsT[:, bass.ts(i, UT), :],
                                     start=True, stop=True)
                last.then_inc(r_done, 1)

            def O(i, k, first, last_unit):
                n = NO * i + k
                pe.wait_ge(onehot_ready, n + 1)
                if not (first and k < 2):
                    pe.wait_ge(o_copied, n - 1)
                r = k // 2 + 2
                indices_follow = k % 2 and (r < RP or not last_unit)
                if indices_follow:
                    pe.wait_ge(index_ready, RP * i + k // 2 + 2)
                for c in range(chunks[k]):
                    for part in (high, low):
                        last = pe.matmul(half(psO[k % 2], 0), part[:, first_chunk[k] + c, :], onehot[k % 2][:, c, :],
                                         start=(c == 0 and part is high), stop=(c == chunks[k] - 1 and part is low))
                last.then_inc(o_done, 1)
                if indices_follow:
                    R(i + r // RP, r % RP)

            def G(i, u, s, first):
                t = UT * i + u
                if s == 0:
                    pe.wait_ge(et_dve, TH * t + TH)
                    pe.wait_ge(et_act, TH * t + TH)
                    pe.wait_ge(o_copied, NO * i + NO)
                if not (first and s < 2):
                    pe.wait_ge(gs_dve, NS * t + s - 1)
                    pe.wait_ge(gs_act, NS * t + s - 1)
                for m in range(SG):
                    b = GROUP * (s * SG + m)
                    stationary = ET[:, u, b:b + GROUP, :].rearrange("d b f -> d (b f)")
                    moving = ET[:, u, b:b + GROUP, 0:F]
                    last = pe.matmul(flat(psG[s % 2])[:, m * GROUP * F:(m + 1) * GROUP * F],
                                     stationary, moving, start=True, stop=True)
                last.then_inc(g_done, 1)

            def M(i, m):
                if m == 0:
                    for u in range(UT):
                        pe.wait_ge(z_landed[u], ZD * i + ZD)
                    wait_since(pe, y_ready, i)
                else:
                    pe.wait_ge(relu_done, RELUS * i + m)
                if m < C1:
                    for c in range(K1):
                        n = weight_rows(c)
                        last = pe.matmul(half(psM, 0), W1_sb[0:n, c, m * P:(m + 1) * P], Z[0:n, c, :],
                                         start=(c == 0), stop=(c == K1 - 1))
                elif m < C1 + C2:
                    for c in range(C1):
                        last = pe.matmul(half(psM, 0), W2_sb[:, c, (m - C1) * P:(m - C1 + 1) * P], h1[:, c, :],
                                         start=(c == 0), stop=(c == C1 - 1))
                else:
                    for c in range(C2):
                        last = pe.matmul(half(psM, 0)[0:1, :], W3_sb[:, c:c + 1], h2[:, c, :],
                                         start=(c == 0), stop=(c == C2 - 1))
                last.then_inc(m_done, 1)

            pe.wait_ge(rows_t_dve, RG)
            pe.wait_ge(select_ready, 1)
            R(0, 0)
            pe.wait_ge(index_ready, 1)
            R(0, 1)

            def unit(i, first=False, last_unit=False):
                for step, n in PHASE_A:
                    if step == "T":
                        T(i, 0, n, first)
                    elif step == "O":
                        O(i, n, first, last_unit)
                    elif not first:
                        G(i - 1, 1, n, False)
                for step, n in PHASE_B:
                    if step == "T":
                        T(i, 1, n, False)
                    elif step == "G":
                        G(i, 0, n, first)
                    elif not first:
                        M(i - 1, n)

            unit(0, first=True)
            pe.wait_ge(weights_landed, DMA * WEIGHT_DMAS)
            unit(1)
            with pe.Fori(2, UNITS - 1) as i:
                unit(i)
            unit(UNITS - 1, last_unit=True)
            for s in range(NS):
                G(UNITS - 1, 1, s, False)
            for m in range(MS):
                M(UNITS - 1, m)

        def copy_et(eng, copy, i, u, q, first, done):
            t = UT * i + u
            f0, step, count = GATHERED[q]
            eng.wait_ge(t_done, NT * t + q + 1)
            if not first:
                eng.wait_ge(g_done, NS * (t - UT) + NS)
            dst = ET[:, u, :, f0:f0 + step * (count - 1) + 1:step].rearrange("d p f -> d f p")
            copy(dst, psT[q % 2][:, 0:count, :]).then_inc(done, 1)

        def copy_gs(eng, copy, i, u, s, quarters, done):
            t = UT * i + u
            if s == 0:
                wait_since(eng, rows_landed[u], DMA * len(BLOCKS) * i)
            eng.wait_ge(g_done, NS * t + s + 1)
            for g in quarters:
                block = flat(psG[s % 2])[QP * g:QP * g + F, g * F:]
                src = bass.AP(tensor=block.tensor, offset=block.offset + F - 1,
                              ap=[list(block.ap[0]), [GROUP * F, SG], [-1, F]])
                dst = Gs[u][:, :, s * SG * GROUP:(s + 1) * SG * GROUP]\
                    .rearrange("i j (n c) -> i n j c", c=GROUP)[:, :, :, g]
                last = copy(dst, src)
            last.then_inc(done, 1)

        @block.vector
        def _(dve):
            dve.memset(rows[:, :, F:QP], 0.0)
            dve.wait_ge(ids_landed, DMA)
            for u in range(UT):
                dve.tensor_copy(idx[:, u, :], ids_sb[:, u, :]).then_inc(idx_ready, 1)
            dve.tensor_copy(rows[:, :, 0:F], ids_sb[:]).then_inc(rows_ready, 1)
            dve.memset(ET[:, :, :, F:], 0.0)
            dve.wait_ge(ident_ready, 1)
            for k, f in enumerate(ONEHOT):
                last = dve.tensor_copy(select[:, k, :], ident[0:F, f:f + 1].to_broadcast([F, VR]))
            last.then_inc(select_ready, 1)
            dve.wait_ge(numbers_made, len(kinds))
            for n in range(len(kinds)):
                last = dve.tensor_copy(numberf[n][:], number[n][:])
            last.then_inc(numbers_made, 1)
            for g in range(RG):
                dve.wait_ge(rows_t_done, g + 1)
                dve.tensor_copy(idsT[:, 4 * g:4 * g + 4, :], row_banks[g][0:F, :, :]).then_inc(rows_t_dve, 1)

            def split_low(k):
                c0, c = first_chunk[k], chunks[k]
                dve.wait_ge(high_ready, k + 1)
                dve.tensor_tensor(low[:, c0:c0 + c, :], raw[k % 2][:, 0:c, :],
                                  high[:, c0:c0 + c, :].bitcast(F32), ALU.subtract).then_inc(low_ready, 1)

            def H(i, k, first=False):
                n = NO * i + k
                dve.wait_ge(index_ready, RP * i + k // 2 + 1)
                if not first:
                    dve.wait_ge(o_done, n - 1)
                for c in range(chunks[k]):
                    last = dve.tensor_scalar(onehot[k % 2][:, c, :], index[:, k // 2 % 2, k % 2, :],
                                             numberf[kinds.index(chunks[k])][:, c:c + 1], None, ALU.is_equal)
                last.then_inc(onehot_ready, 1)

            dve.wait_ge(numbers_made, len(kinds) + 1)
            for k in range(2):
                split_low(k)
                H(0, k, True)

            def unit(i, first=False, last_unit=False):
                for step, n in PHASE_A:
                    if step == "T" and n % 2 == 0:
                        copy_et(dve, dve.tensor_copy, i, 0, n, first, et_dve)
                    elif step == "T" and n == NT - 1:
                        next_indices(i, 0, last_unit)
                    elif step == "O":
                        if first and n + 2 < NO:
                            split_low(n + 2)
                        if n + 2 < NO:
                            H(i, n + 2)
                        elif not last_unit:
                            H(i + 1, n + 2 - NO)
                    elif step == "G" and not first:
                        copy_gs(dve, dve.tensor_copy, i - 1, 1, n, VQ, gs_dve)
                for step, n in PHASE_B:
                    if step == "T" and n % 2 == 0:
                        copy_et(dve, dve.tensor_copy, i, 1, n, first, et_dve)
                    elif step == "T" and n == NT - 1:
                        next_indices(i, 1, last_unit)
                    elif step == "G":
                        copy_gs(dve, dve.tensor_copy, i, 0, n, VQ, gs_dve)
                    elif step == "M" and n == MS - 1 and not first:
                        write_y(i - 1)

            def next_indices(i, u, last_unit):
                if not last_unit:
                    dve.wait_ge(t_done, NT * (UT * i + u) + NT)
                    dve.tensor_copy(idx[:, u:u + 1, :], ids_sb[:, bass.ts(UT * (i + 1) + u, 1), :])\
                       .then_inc(idx_ready, 1)

            def write_y(i):
                dve.wait_ge(m_done, MS * i + MS)
                dve.tensor_copy(y_sb[:, :, bass.ds(UT * i, UT)].rearrange("o p t -> o t p"),
                                half(psM, 0)[0:1, :].rearrange("o (t p) -> o t p", t=UT)).then_inc(y_ready, 1)

            unit(0, first=True)
            unit(1)
            with dve.Fori(2, UNITS - 1) as i:
                unit(i)
            unit(UNITS - 1, last_unit=True)
            for s in range(NS):
                copy_gs(dve, dve.tensor_copy, UNITS - 1, 1, s, VQ, gs_dve)
            write_y(UNITS - 1)

        @block.scalar
        def _(act):
            def split_high(k):
                c0, c = first_chunk[k], chunks[k]
                act.wait_ge(raw_landed[k % 2], DMA * (k // 2 + 1))
                act.copy(high[:, c0:c0 + c, :], raw[k % 2][:, 0:c, :]).then_inc(high_ready, 1)

            def copy_o(i, k, first):
                n = NO * i + k
                act.wait_ge(o_done, n + 1)
                if not first:
                    act.wait_ge(g_done, NS * UT * i)
                act.copy(ET[:, :, :, ONEHOT[k]], half(psO[k % 2], 0).rearrange("d (u p) -> d u p", u=UT))\
                   .then_inc(o_copied, 1)

            def copy_index(i, r, first=False):
                n = RP * i + r
                act.wait_ge(r_done, n + 1)
                if not first:
                    act.wait_ge(onehot_ready, 2 * n - 2)
                act.copy(index[:, r % 2, :, :], flat(psR)[0:VR, :].rearrange("v (n b) -> v n b", n=2))\
                   .then_inc(index_ready, 1)

            def relu(i, m):
                act.wait_ge(m_done, MS * i + m + 1)
                h, n, b = (h1, m, b1_sb) if m < C1 else (h2, m - C1, b2_sb)
                act.activation(h[:, n, :], half(psM, 0), ACT.Relu, bias=b[:, n:n + 1]).then_inc(relu_done, 1)

            split_high(0)
            for g in range(RG):
                act.wait_ge(rows_t_done, g + 1)
                act.copy(denseT[:, 4 * g:4 * g + 4, :], row_banks[g][QP:QP + ND, :, :]).then_inc(rows_t_act, 1)
            split_high(1)
            copy_index(0, 0, True)
            copy_index(0, 1, True)

            def unit(i, first=False, last_unit=False):
                for step, n in PHASE_A:
                    if step == "T" and n % 2:
                        copy_et(act, act.copy, i, 0, n, first, et_act)
                    elif step == "O":
                        if first and n + 2 < NO:
                            split_high(n + 2)
                        copy_o(i, n, first)
                        r = n // 2 + 2
                        if n % 2 and r < RP:
                            copy_index(i, r)
                        elif n % 2 and not last_unit:
                            copy_index(i + 1, r - RP)
                    elif step == "G" and not first:
                        copy_gs(act, act.copy, i - 1, 1, n, AQ, gs_act)
                for step, n in PHASE_B:
                    if step == "T" and n % 2:
                        copy_et(act, act.copy, i, 1, n, first, et_act)
                    elif step == "G":
                        copy_gs(act, act.copy, i, 0, n, AQ, gs_act)
                    elif step == "M" and n < RELUS and not first:
                        relu(i - 1, n)

            unit(0, first=True)
            act.wait_ge(weights_landed, DMA * WEIGHT_DMAS)
            unit(1)
            with act.Fori(2, UNITS - 1) as i:
                unit(i)
            unit(UNITS - 1, last_unit=True)
            for s in range(NS):
                copy_gs(act, act.copy, UNITS - 1, 1, s, AQ, gs_act)
            for m in range(RELUS):
                relu(UNITS - 1, m)


def kernel(**inputs):
    import numpy as np
    import concourse.bacc as bacc
    from concourse.bass_utils import run_bass_kernel_spmd

    nc = bacc.Bacc("TRN2", target_bir_lowering=False, num_devices=1)
    arrays, aps = {}, {}
    for name, value in inputs.items():
        if name == "W_top1":
            value = np.asarray(value)[weight_order(inputs["ids"].shape[1], value.shape[0])]
        arrays[f"in_{name}"] = np.ascontiguousarray(value)
        a = arrays[f"in_{name}"]
        aps[name] = nc.dram_tensor(f"in_{name}", a.shape, mybir.dt.from_np(a.dtype), kind="ExternalInput").ap()
    batch, features = inputs["ids"].shape
    out = nc.dram_tensor("y_out", (batch, 1), F32, kind="ExternalOutput").ap()
    dlrm_tower(nc, aps["dense_ctx"], aps["ids"], [aps[f"tbl_{f}"] for f in range(features)],
               aps["W_top1"], aps["b_top1"], aps["W_top2"], aps["b_top2"], aps["W_top3"], out)
    result = run_bass_kernel_spmd(nc, [arrays], core_ids=[0])
    return result.results[0]["y_out"]
```

```python
from contextlib import ExitStack

import concourse.bass as bass
from concourse import mybir

ALU = mybir.AluOpType
ACT = mybir.ActivationFunctionType
F32 = mybir.dt.float32
F32R = mybir.dt.float32r
F16 = mybir.dt.float16
I32 = mybir.dt.int32

P = 128
DMA = 16
SPLIT_ROWS = 125
ONEHOT = (4, 12, 16, 19, 22, 25, 24, 26)
GATHERED = ((0, 1, 4), (5, 1, 4), (9, 1, 3), (13, 1, 3), (17, 3, 3), (18, 3, 2))


def weight_order(F, rows):
    pair = {}
    for i in range(F):
        for j in range(i + 1, F):
            pair[i, j] = len(pair)
    order = [pair[min(i, (i + s) % F), max(i, (i + s) % F)]
             for s in range(F // 2, 0, -1) for i in range(F - 1, -1, -1)]
    return order + list(range(len(pair), rows))


def dlrm_tower(nc, dense_ctx, ids, tables, W1, b1, W2, b2, W3, out):
    batch, F = ids.shape
    D = tables[0].shape[1]
    ND = dense_ctx.shape[1]
    H1, H2 = W1.shape[1], W2.shape[1]
    TILES = batch // P
    UT = 2
    UNITS = TILES // UT
    UB = UT * P
    GROUP = 4
    QP = P // GROUP
    PAIRS = F * (F - 1) // 2
    K1 = -(-(PAIRS + ND) // P)
    C1, C2 = H1 // P, H2 // P
    assert D == P and F <= QP and PAIRS + ND == W1.shape[0] and TILES % UT == 0

    TG = [[f0 + step * n for n in range(count)] for f0, step, count in GATHERED]
    NT = len(TG)
    TH = NT // 2
    assert NT % 2 == 0 and sorted(sum(TG, []) + list(ONEHOT)) == list(range(F))
    slot_of = {f: n for n, f in enumerate(sum(TG, []))}
    EXTRA = ONEHOT[-2:]
    for f in EXTRA:
        slot_of[f] = len(slot_of)
    NF = len(slot_of)

    NO = len(ONEHOT)
    VR = SPLIT_ROWS
    chunks = [tables[f].shape[0] // VR for f in ONEHOT]
    first_chunk = [sum(chunks[:n]) for n in range(NO)]
    CMAX = max(chunks)
    kinds = sorted(set(chunks))
    RP = NO // 2
    CH = CMAX // 2
    assert all(tables[f].shape[0] % (2 * VR) == 0 and tables[f].shape[0] < 2048 for f in ONEHOT)
    assert NO % 4 == 0 and all(chunks[2 * r] == chunks[2 * r + 1] for r in range(RP))

    SG = 4
    NS = P // GROUP // SG

    S = F // 2
    assert F % 2 and S * F == PAIRS
    BLOCKS = ((0, S + 1, 1, F, 0), (S + 1, F, S + 2, F, 0), (S + 1, F, 0, S, 1))
    DRAM_ROWS = F * (S + 2 * F)
    Z_START = F * F - S * F - (F - 1)
    dense_row = PAIRS - (K1 - 1) * P
    assert 0 < dense_row and dense_row + ND <= P
    ZD = 3 * DMA
    MS = C1 + C2 + 1
    RELUS = C1 + C2

    def steps(line):
        return [(step[0], int(step[1])) for step in line.split()]

    PHASE_A = steps("T0 O0 G0 G1 G2 T1 G3 Z0 G4 O1 G5 T2 G6 G7 O2 C0 T3 O3 C1 O4 T4 O5 C2 T5 O6 Z1 O7 C3")
    PHASE_B = steps("T0 M0 M1 G0 G1 T1 M2 G2 M3 T2 G3 H0 G4 T3 M4 G5 M5 G6 T4 G7 M6 T5 H1")
    LAST_A = steps("T0 O0 G0 G1 G2 T1 G3 Z0 G4 O1 G5 T2 G6 G7 O2 C0 T3 O3 C1 O4 T4 O5 C2 T5 X0 Z1")
    LAST_B = steps("T0 T1 G0 T2 G1 T3 G2 G3 T4 G4 T5 G5 X1 G6 G7")
    FIRST_A = steps("O0 O1 C0 T0 T1 O2 T2 O3 C1 T3 O4 T4 O5 C2 T5 O6 O7 C3")
    FIRST_B = steps("T0 G0 G1 T1 G2 H0 G3 T2 G4 H1 G5 T3 G6 T4 G7 T5")
    TAIL = [(UNITS - 2, m) for m in range(MS - 1)] + [(UNITS - 1, 0), (UNITS - 1, 1), (UNITS - 2, MS - 1)] + \
           [(UNITS - 1, m) for m in range(2, MS)]
    SPLIT_BEFORE = [(UNITS - 2, C1), (UNITS - 2, C1 + 1)]

    def count_off(name, count):
        return [(name, n) for n in range(count)]

    g_steps, z_steps = count_off("G", NS), count_off("Z", UT)
    of_first = 2 * count_off("T", NT) + count_off("O", 2 * RP) + count_off("C", RP) + g_steps + count_off("H", 2)
    of_last = 2 * count_off("T", NT) + count_off("O", 2 * RP - 2) + count_off("C", RP - 1) + 2 * g_steps + z_steps
    assert sorted(FIRST_A + FIRST_B) == sorted(of_first)
    assert sorted(PHASE_A + PHASE_B) == sorted(of_first + g_steps + z_steps + count_off("M", MS))
    assert sorted(LAST_A + LAST_B) == sorted(of_last + count_off("X", UT))

    with ExitStack() as ctx:
        def sb(name, shape, dt=F32):
            return ctx.enter_context(nc.sbuf_tensor(name, shape, dt))

        def bank(name):
            return ctx.enter_context(nc.psum_tensor(name, [P, 4, P], F32))

        def sem(name):
            return ctx.enter_context(nc.semaphore(name))

        ids_sb = sb("ids_sb", [P, TILES, F], I32)
        idx = sb("idx", [P, UT, F], I32)
        idsT = sb("idsT", [NO, TILES, P], F16)
        wide = sb("wide", [P, TILES * P])
        denseT = wide[0:ND, :].rearrange("d (t p) -> d t p", t=TILES)
        y_sb = wide[QP:QP + 1, :].rearrange("o (p t) -> o p t", t=TILES)
        W1_sb = [sb(f"W1_sb{n}", [P, K1, H1], F32R) for n in range(2)]
        W2_sb = [sb(f"W2_sb{n}", [P, C1, H2], F32R) for n in range(2)]
        W3_sb = [sb(f"W3_sb{n}", [P, C2], F32R) for n in range(2)]
        W3_raw = sb("W3_raw", [P, C2])
        b1_sb = sb("b1_sb", [P, C1])
        b2_sb = sb("b2_sb", [P, C2])
        ident = sb("ident", [P, P])
        number = [sb(f"number{c}", [VR, c], I32) for c in kinds]
        numberf = [sb(f"numberf{c}", [VR, c]) for c in kinds]
        high = sb("high", [VR, sum(chunks), D], F32R)
        low = sb("low", [VR, sum(chunks), D], F32R)
        index = sb("index", [VR, NO, UB], F16)
        onehot = [sb(f"onehot{n}", [VR, 2, CH, UB], F32R) for n in range(2)]
        E = sb("E", [P, NF, D])
        ET = sb("ET", [P, UT, P, QP])
        Gs_all = sb("Gs_all", [P, F, P])
        Gs = [Gs_all[P // UT * u:P // UT * u + F, :, :] for u in range(UT)]
        RAW = F // CH
        raw = [Gs_all[0:VR, n * CH:(n + 1) * CH, :] for n in range(RAW)]
        spread_rows = [nc.dram_tensor(f"spread_rows{u}", [DRAM_ROWS, P], F32, kind="Internal").ap() for u in range(UT)]
        ids_rows = nc.dram_tensor("ids_rows", [UNITS, NO * UB], F16, kind="Internal").ap()
        whole = sb("whole", [P, K1 * H1])
        rows = whole[:, 0:TILES * (QP + ND)].rearrange("p (t c) -> p t c", t=TILES)
        W1_raw = whole[:, :].rearrange("p (c n) -> p c n", c=K1)
        W2_raw = whole[:, 0:C1 * H2].rearrange("p (c n) -> p c n", c=C1)
        Z = whole[:, 0:K1 * UB].rearrange("p (c b) -> p c b", c=K1)
        hidden = whole[:, K1 * UB:(K1 + 2) * UB].rearrange("p (n b) -> p n b", n=2)
        Zs = [sb(f"Zs{n}", [P, K1, UB], F32R) for n in range(2)]
        h1 = [sb(f"h1_{n}", [P, C1, UB], F32R) for n in range(2)]
        h2 = [sb(f"h2_{n}", [P, C2, UB], F32R) for n in range(2)]

        psT = [bank(f"psT{n}") for n in range(2)]
        psG = [bank(f"psG{n}") for n in range(2)]
        psO = [bank(f"psO{n}") for n in range(2)]
        psM = [bank(f"psM{n}") for n in range(2)]

        def flat(b):
            return b[:, :, :].rearrange("p a b -> p (a b)")

        def half(b, n):
            return flat(b)[:, n * UB:(n + 1) * UB]

        ids_landed = sem("ids_landed")
        dense_landed = sem("dense_landed")
        bias_landed = sem("bias_landed")
        cleared = sem("cleared")
        ident_ready = sem("ident_ready")
        numbers_made = sem("numbers_made")
        rows_ready = sem("rows_ready")
        raw_landed = [sem(f"raw_landed{n}") for n in range(RAW)]
        high_ready = sem("high_ready")
        low_ready = sem("low_ready")
        W_landed = [sem(f"W{n}_landed") for n in (1, 2, 3)]
        W_high = sem("W_high")
        W_low = sem("W_low")
        idx_ready = sem("idx_ready")
        gathered = [sem(f"gathered{q}") for q in range(NT)]
        extra_gathered = sem("extra_gathered")
        x_done = sem("x_done")
        x_copied = sem("x_copied")
        slot_free = sem("slot_free")
        rows_t_done = sem("rows_t_done")
        rows_t_dve = sem("rows_t_dve")
        rows_t_act = sem("rows_t_act")
        t_done = sem("t_done")
        et_dve = sem("et_dve")
        et_act = sem("et_act")
        ids_written = sem("ids_written")
        index_landed = sem("index_landed")
        onehot_ready = sem("onehot_ready")
        o_done = sem("o_done")
        o_copied = sem("o_copied")
        g_done = sem("g_done")
        gs_copied = sem("gs_copied")
        rows_landed = [sem(f"rows_landed{u}") for u in range(UT)]
        z_landed = [sem(f"z_landed{u}") for u in range(UT)]
        z_high = sem("z_high")
        z_low = sem("z_low")
        m_done = sem("m_done")
        y_done = sem("y_done")
        relu_done = sem("relu_done")
        relu_low = sem("relu_low")
        y_ready = sem("y_ready")
        out_landed = sem("out_landed")

        block = ctx.enter_context(nc.Block())

        def wait_since(eng, semaphore, count):
            if not (isinstance(count, int) and count <= 0):
                eng.wait_ge(semaphore, count)

        row_banks = [psT[0], psT[1], psG[0], psG[1]]
        o_banks = [psO, psM]
        RG = TILES // 4
        assert RG == len(row_banks)

        QUARTERS = 2 * NO

        def quarter(n):
            table = n // 4 * 2 + n % 2
            count = chunks[table] // 2
            return table, n // 2 % 2 * count, count

        def weight_rows(c):
            return min(P, W1.shape[0] - c * P)

        @block.sync
        def _(sp):
            sp.dma_start(ids_sb[:], ids.rearrange("(p t) f -> p t f", t=TILES)).then_inc(ids_landed, DMA)

            def load_quarter(n):
                table, c0, count = quarter(n)
                if n >= RAW:
                    sp.wait_ge(low_ready, n - RAW + 1)
                sp.dma_start(raw[n % RAW][:, 0:count, :],
                             tables[ONEHOT[table]].rearrange("(p c) d -> p c d", p=VR)[:, c0:c0 + count, :])\
                  .then_inc(raw_landed[n % RAW], DMA)

            load_quarter(0)
            sp.dma_start(rows[:, :, QP:], dense_ctx.rearrange("(p t) f -> p t f", t=TILES)).then_inc(dense_landed, DMA)
            for n in range(1, RAW):
                load_quarter(n)
            with nc.allow_non_contiguous_dma("vectors, once"):
                sp.dma_start(W3_raw[:], W3.rearrange("(c p) n -> p (c n)", p=P)).then_inc(W_landed[2], DMA)
                sp.dma_start(b1_sb[:], b1.rearrange("(c p) -> p c", p=P)).then_inc(bias_landed, DMA)
                sp.dma_start(b2_sb[:], b2.rearrange("(c p) -> p c", p=P)).then_inc(bias_landed, DMA)

            def write_ids(g0, g1):
                sp.wait_ge(rows_t_dve, g1)
                t0, t1 = 4 * g0, 4 * g1
                sp.dma_start(ids_rows[t0 // UT:t1 // UT, :].rearrange("i (k b) -> k i b", k=NO),
                             idsT[:, t0:t1, :].rearrange("k (i u) p -> k i (u p)", u=UT)).then_inc(ids_written, DMA)

            def load_index(i, first=False):
                if not first:
                    sp.wait_ge(onehot_ready, 2 * RP * i)
                sp.dma_start(index[:].rearrange("v k b -> v (k b)"),
                             ids_rows[bass.ds(i, 1), :].to_broadcast([VR, NO * UB])).then_inc(index_landed, DMA)

            write_ids(0, 1)
            sp.wait_ge(ids_written, DMA)
            load_index(0, True)
            write_ids(1, RG)
            for n in range(RAW, QUARTERS):
                load_quarter(n)
            sp.wait_ge(rows_t_dve, RG)
            sp.wait_ge(rows_t_act, RG)
            last_chunk = (K1 - 1) * P
            sp.dma_start(W1_raw[:, 0:K1 - 1, :], W1[0:last_chunk, :].rearrange("(c p) n -> p c n", p=P))\
              .then_inc(W_landed[0], DMA)
            sp.dma_start(W1_raw[0:weight_rows(K1 - 1), K1 - 1, :], W1[last_chunk:, :]).then_inc(W_landed[0], DMA)
            sp.wait_ge(ids_written, 2 * DMA)
            load_index(1)
            sp.wait_ge(W_low, 1)
            sp.dma_start(W2_raw, W2.rearrange("(c p) n -> p c n", p=P)).then_inc(W_landed[1], DMA)
            sp.wait_ge(W_low, 2)

            def scatter_tile(i, u, first):
                t = UT * i + u
                if not first:
                    sp.wait_ge(z_landed[u], ZD * i)
                sp.wait_ge(gs_copied, NS * t + NS)
                for i0, i1, j0, j1, wrap in BLOCKS:
                    scratch = spread_rows[u]
                    start = F * F - (j1 - 1 - i0 + wrap * F) * F - i0
                    dst = bass.AP(tensor=scratch.tensor, offset=scratch.offset + start * P,
                                  ap=[[(F - 1) * P, i1 - i0], [F * P, j1 - j0], [1, P]])
                    sp.dma_start(dst, Gs[u][i0:i1, F - j1:F - j0, :]).then_inc(rows_landed[u], DMA)
                if not first:
                    sp.wait_ge(z_low, UT * (i - 1) + u + 1)
                sp.dma_start(Z[dense_row:dense_row + ND, K1 - 1, u * P:(u + 1) * P], denseT[:, bass.ts(t, 1), :])\
                  .then_inc(z_landed[u], DMA)
                sp.wait_ge(rows_landed[u], DMA * len(BLOCKS) * (i + 1))
                last_chunk = Z_START + (K1 - 1) * P
                sp.dma_start(Z[:, 0:K1 - 1, u * P:(u + 1) * P],
                             spread_rows[u][Z_START:last_chunk, :].rearrange("(c p) b -> p c b", p=P))\
                  .then_inc(z_landed[u], DMA)
                sp.dma_start(Z[0:dense_row, K1 - 1, u * P:(u + 1) * P],
                             spread_rows[u][last_chunk:last_chunk + dense_row, :]).then_inc(z_landed[u], DMA)

            for u in range(UT):
                scatter_tile(0, u, True)
            with sp.Fori(1, UNITS - 1) as i:
                load_index(i + 1)
                for u in range(UT):
                    scatter_tile(i, u, False)
            for u in range(UT):
                scatter_tile(UNITS - 1, u, False)
            sp.wait_ge(y_ready, UNITS)
            sp.dma_start(out.rearrange("b o -> o b"), y_sb.rearrange("o p t -> o (p t)")).then_inc(out_landed, DMA)
            sp.wait_ge(out_landed, DMA)

        @block.gpsimd
        def _(pool):
            def gather_tile(i, u, first_unit=False, last_unit=False):
                t = UT * i + u
                first = first_unit and u == 0
                if first_unit:
                    pool.wait_ge(ids_landed, DMA)
                    tile_ids = ids_sb[:, u, :]
                else:
                    pool.wait_ge(idx_ready, t + 1 - UT)
                    tile_ids = idx[:, u, :]
                pool.sem_inc(slot_free, 1)
                for q, group in enumerate(TG):
                    if not first:
                        pool.wait_ge(t_done, NT * (t - 1) + q + 1)
                        pool.sem_inc(slot_free, 1)
                    for f in group:
                        pool.indirect_dma_start(
                            E[:, slot_of[f], :], None, tables[f],
                            bass.IndirectOffsetOnAxis(ap=tile_ids[:, f:f + 1], axis=0),
                        ).then_inc(gathered[q], DMA)
                if last_unit:
                    if u:
                        pool.wait_ge(x_done, u)
                        pool.sem_inc(slot_free, 1)
                    for f in EXTRA:
                        pool.indirect_dma_start(
                            E[:, slot_of[f], :], None, tables[f],
                            bass.IndirectOffsetOnAxis(ap=tile_ids[:, f:f + 1], axis=0),
                        ).then_inc(extra_gathered, DMA)

            pool.memset(ident[:], 0.0).then_inc(cleared, 1)
            pool.wait_ge(cleared, 1)
            pool.affine_select(out=ident[:], in_=ident[:], compare_op=ALU.not_equal, fill=1.0, base=0,
                               pattern=[[-1, P]], channel_multiplier=1).then_inc(ident_ready, 1)
            for n, c in enumerate(kinds):
                pool.iota(number[n][:], pattern=[[1, c]], base=0, channel_multiplier=c).then_inc(numbers_made, 1)
            for u in range(UT):
                gather_tile(0, u, first_unit=True)
            with pool.Fori(1, UNITS - 1) as i:
                for u in range(UT):
                    gather_tile(i, u)
            for u in range(UT):
                gather_tile(UNITS - 1, u, last_unit=True)

        @block.tensor
        def _(pe):
            pe.wait_ge(ident_ready, 1)
            pe.wait_ge(rows_ready, 1)
            pe.wait_ge(dense_landed, DMA)
            for g in range(RG):
                for n in range(4):
                    last = pe.transpose(row_banks[g][0:QP + ND, n, :], rows[:, 4 * g + n, :], ident[:])
                last.then_inc(rows_t_done, 1)

            def T(i, u, q, first):
                t = UT * i + u
                pe.wait_ge(gathered[q], DMA * len(TG[q]) * (t + 1))
                if q >= 2 or not first:
                    pe.wait_ge(et_act if q % 2 else et_dve, TH * t + q // 2)
                else:
                    pe.wait_ge(rows_t_dve, RG)
                    pe.wait_ge(rows_t_act, RG)
                for n, f in enumerate(TG[q]):
                    last = pe.transpose(psT[q % 2][:, n, :], E[:, slot_of[f], :], ident[:])
                last.then_inc(t_done, 1)

            def X(u):
                pe.wait_ge(extra_gathered, DMA * len(EXTRA) * (u + 1))
                pe.wait_ge(o_copied, RP * (UNITS - 1) + 2)
                for n, f in enumerate(EXTRA):
                    last = pe.transpose(psM[u][:, n, :], E[:, slot_of[f], :], ident[:])
                last.then_inc(x_done, 1)

            def O(i, h, first):
                n = 2 * RP * i + h
                r = h // 2
                banks = o_banks[r % 2]
                pe.wait_ge(onehot_ready, n + 1)
                if first:
                    pe.wait_ge(low_ready, 2 * h + 2)
                if h % 2 == 0:
                    wait_since(pe, o_copied, RP * i + r - 1)
                    if r == 0:
                        wait_since(pe, relu_done, RELUS * (i - 1))
                    elif r == 1:
                        wait_since(pe, y_ready, i - 1)
                count = chunks[2 * r] // 2
                for k in range(2):
                    table = 2 * r + k
                    for c in range(count):
                        chunk = first_chunk[table] + count * (h % 2) + c
                        for part in (high, low):
                            last = pe.matmul(half(banks[k], 0), part[:, chunk, :], onehot[h % 2][:, k, c, :],
                                             start=(h % 2 == 0 and c == 0 and part is high),
                                             stop=(h % 2 == 1 and c == count - 1 and part is low))
                last.then_inc(o_done, 1)

            def G(i, u, s, first=False, last_unit=False):
                t = UT * i + u
                if s == 0:
                    pe.wait_ge(et_dve, TH * t + TH)
                    pe.wait_ge(et_act, TH * t + TH)
                    if last_unit:
                        pe.wait_ge(o_copied, RP * i + RP - 1)
                        pe.wait_ge(x_copied, u + 1)
                    else:
                        pe.wait_ge(o_copied, RP * i + RP)
                if not (first and s < 2):
                    pe.wait_ge(gs_copied, NS * t + s - 1)
                for m in range(SG):
                    b = GROUP * (s * SG + m)
                    stationary = ET[:, u, b:b + GROUP, :].rearrange("d b f -> d (b f)")
                    moving = ET[:, u, b:b + GROUP, 0:F]
                    last = pe.matmul(flat(psG[s % 2])[:, m * GROUP * F:(m + 1) * GROUP * F],
                                     stationary, moving, start=True, stop=True)
                last.then_inc(g_done, 1)

            def products(out_, weights, values, begins, ends):
                for w, v in ((0, 0), (0, 1), (1, 0)):
                    last = pe.matmul(out_, weights(w), values(v), start=(begins and (w, v) == (0, 0)),
                                     stop=(ends and (w, v) == (1, 0)))
                return last

            def M(i, m, tail=False):
                if m == 0:
                    pe.wait_ge(z_low, UT * i + UT)
                    pe.wait_ge(o_copied, RP * (UNITS if tail else i + 2) - 1)
                if m >= 2 or (tail and i == UNITS - 1):
                    pe.wait_ge(relu_done, RELUS * i + m - 1)
                if m < C1:
                    for c in range(K1):
                        n = weight_rows(c)
                        last = products(half(psO[m % 2], 0), lambda w: W1_sb[w][0:n, c, m * P:(m + 1) * P],
                                        lambda v: Zs[v][0:n, c, :], c == 0, c == K1 - 1)
                elif m < C1 + C2:
                    for c in range(C1):
                        if m == C1:
                            pe.wait_ge(relu_low, RELUS * i + c + 1)
                        last = products(half(psO[m % 2], 0), lambda w: W2_sb[w][:, c, (m - C1) * P:(m - C1 + 1) * P],
                                        lambda v: h1[v][:, c, :], c == 0, c == C1 - 1)
                else:
                    if tail:
                        pe.wait_ge(x_copied, UT)
                        pe.wait_ge(y_ready, i)
                    else:
                        pe.wait_ge(o_copied, RP * (i + 2))
                    for c in range(C2):
                        pe.wait_ge(relu_low, RELUS * i + C1 + c + 1)
                        last = products(half(psM[0], 0)[0:1, :], lambda w: W3_sb[w][:, c:c + 1],
                                        lambda v: h2[v][:, c, :], c == 0, c == C2 - 1)
                last.then_inc(m_done if m < RELUS else y_done, 1)

            def unit(i, first=False, last_unit=False):
                for step, n in FIRST_A if first else LAST_A if last_unit else PHASE_A:
                    if step == "T":
                        T(i, 0, n, first)
                    elif step == "X":
                        X(0)
                    elif step == "O":
                        O(i, n, first)
                    elif step == "G":
                        G(i - 1, 1, n)
                for step, n in FIRST_B if first else LAST_B if last_unit else PHASE_B:
                    if step == "T":
                        T(i, 1, n, False)
                    elif step == "X":
                        X(1)
                    elif step == "G":
                        G(i, 0, n, first, last_unit)
                    elif step == "M":
                        M(i - 1, n)

            unit(0, first=True)
            pe.wait_ge(W_low, 3)
            unit(1)
            with pe.Fori(2, UNITS - 1) as i:
                unit(i)
            unit(UNITS - 1, last_unit=True)
            for s in range(NS):
                G(UNITS - 1, 1, s, last_unit=True)
            for i, m in TAIL:
                M(i, m, tail=True)

        z_pieces = [(slice(0, K1 - 1), P), (slice(K1 - 1, K1), weight_rows(K1 - 1))]
        weight_parts = [
            [(W1_raw, W1_sb, lambda w, cs=cs, n=n: w[0:n, cs, :]) for cs, n in z_pieces],
            [(W2_raw, W2_sb, lambda w: w[:, :, :])],
            [(W3_raw, W3_sb, lambda w: w[:, :])],
        ]

        def copy_et(eng, copy, i, u, q, first, done):
            t = UT * i + u
            f0, step, count = GATHERED[q]
            eng.wait_ge(t_done, NT * t + q + 1)
            if not first:
                eng.wait_ge(g_done, NS * (t - UT) + NS)
            dst = ET[:, u, :, f0:f0 + step * (count - 1) + 1:step].rearrange("d p f -> d f p")
            copy(dst, psT[q % 2][:, 0:count, :]).then_inc(done, 1)

        def copy_gs(act, i, u, s):
            t = UT * i + u
            if s == 0:
                wait_since(act, rows_landed[u], DMA * len(BLOCKS) * i)
            act.wait_ge(g_done, NS * t + s + 1)
            for g in range(GROUP):
                block = flat(psG[s % 2])[QP * g:QP * g + F, g * F:]
                src = bass.AP(tensor=block.tensor, offset=block.offset + F - 1,
                              ap=[list(block.ap[0]), [GROUP * F, SG], [-1, F]])
                dst = Gs[u][:, :, s * SG * GROUP:(s + 1) * SG * GROUP]\
                    .rearrange("i j (n c) -> i n j c", c=GROUP)[:, :, :, g]
                last = act.copy(dst, src)
            last.then_inc(gs_copied, 1)

        @block.vector
        def _(dve):
            dve.memset(rows[:, :, NO:QP], 0.0)
            dve.wait_ge(ids_landed, DMA)
            for r in range(RP):
                f0, f1 = ONEHOT[2 * r:2 * r + 2]
                last = dve.tensor_copy(rows[:, :, 2 * r:2 * r + 2], ids_sb[:, :, f0:f1 + 1:f1 - f0])
            last.then_inc(rows_ready, 1)
            dve.memset(ET[:, :, :, F:], 0.0)
            dve.wait_ge(numbers_made, len(kinds))
            for n in range(len(kinds)):
                last = dve.tensor_copy(numberf[n][:], number[n][:])
            last.then_inc(numbers_made, 1)
            for g in range(RG):
                dve.wait_ge(rows_t_done, g + 1)
                dve.tensor_copy(idsT[:, 4 * g:4 * g + 4, :], row_banks[g][0:NO, :, :]).then_inc(rows_t_dve, 1)

            def split_low(n):
                table, c0, count = quarter(n)
                c0 += first_chunk[table]
                dve.wait_ge(high_ready, n + 1)
                dve.tensor_tensor(low[:, c0:c0 + count, :], raw[n % RAW][:, 0:count, :],
                                  high[:, c0:c0 + count, :].bitcast(F32), ALU.subtract).then_inc(low_ready, 1)

            def H(i, h, first=False):
                n = 2 * RP * i + h
                r = h // 2
                dve.wait_ge(index_landed, DMA * i + DMA)
                if not first:
                    dve.wait_ge(o_done, n - 1)
                count = chunks[2 * r] // 2
                numbers = numberf[kinds.index(chunks[2 * r])]
                for c in range(count):
                    v = count * (h % 2) + c
                    last = dve.tensor_scalar(onehot[h % 2][:, :, c, :], index[:, 2 * r:2 * r + 2, :],
                                             numbers[:, v:v + 1], None, ALU.is_equal)
                last.then_inc(onehot_ready, 1)

            def split_weights_low(n):
                for raw_w, parts, shape in weight_parts[n]:
                    dve.wait_ge(W_high, n + 1)
                    last = dve.tensor_tensor(shape(parts[1]), shape(raw_w), shape(parts[0]).bitcast(F32), ALU.subtract)
                last.then_inc(W_low, 1)

            def split_z_low(i, u):
                dve.wait_ge(z_high, UT * i + u + 1)
                at = slice(u * P, (u + 1) * P)
                for cs, n in z_pieces:
                    last = dve.tensor_tensor(Zs[1][0:n, cs, at], Z[0:n, cs, at], Zs[0][0:n, cs, at].bitcast(F32),
                                             ALU.subtract)
                last.then_inc(z_low, 1)

            def hidden_low(i, m):
                h, n = (h1, m) if m < C1 else (h2, m - C1)
                dve.wait_ge(relu_done, RELUS * i + m + 1)
                dve.tensor_tensor(h[1][:, n, :], hidden[:, m % 2, :], h[0][:, n, :].bitcast(F32), ALU.subtract)\
                   .then_inc(relu_low, 1)

            dve.wait_ge(numbers_made, len(kinds) + 1)
            for h in range(2):
                split_low(2 * h)
                split_low(2 * h + 1)
                H(0, h, True)

            def unit(i, first=False, last_unit=False):
                for step, n in FIRST_A if first else LAST_A if last_unit else PHASE_A:
                    if step == "T" and n % 2 == 0:
                        copy_et(dve, dve.tensor_copy, i, 0, n, first, et_dve)
                    elif step == "X":
                        copy_extra(0)
                    elif step == "T" and n == NT - 1:
                        next_indices(i, 0, last_unit)
                    elif step == "O" and n + 2 < 2 * RP - 2 * last_unit:
                        if first:
                            split_low(2 * n + 4)
                            split_low(2 * n + 5)
                        H(i, n + 2)
                    elif step == "Z":
                        split_z_low(i - 1, n)
                if first:
                    split_weights_low(0)
                for step, n in FIRST_B if first else LAST_B if last_unit else PHASE_B:
                    if step == "T" and n % 2 == 0:
                        copy_et(dve, dve.tensor_copy, i, 1, n, first, et_dve)
                    elif step == "X":
                        copy_extra(1)
                    elif step == "T" and n == NT - 1:
                        next_indices(i, 1, last_unit)
                    elif step == "H":
                        H(i + 1, n)
                    elif step == "M":
                        if n < RELUS:
                            hidden_low(i - 1, n)
                        else:
                            write_y(i - 1)
                if first:
                    split_weights_low(1)
                    split_weights_low(2)

            def copy_extra(u):
                dve.wait_ge(x_done, u + 1)
                dve.wait_ge(g_done, NS * UT * (UNITS - 1))
                f0, f1 = EXTRA
                dve.tensor_copy(ET[:, u, :, f0:f1 + 1:f1 - f0].rearrange("d p f -> d f p"), psM[u][:, 0:2, :])\
                   .then_inc(x_copied, 1)

            def next_indices(i, u, last_unit):
                if not last_unit:
                    dve.wait_ge(t_done, NT * (UT * i + u) + NT)
                    dve.tensor_copy(idx[:, u:u + 1, :], ids_sb[:, bass.ts(UT * (i + 1) + u, 1), :])\
                       .then_inc(idx_ready, 1)

            def write_y(i):
                dve.wait_ge(y_done, i + 1)
                dve.tensor_copy(y_sb[:, :, bass.ds(UT * i, UT)].rearrange("o p t -> o t p"),
                                half(psM[0], 0)[0:1, :].rearrange("o (t p) -> o t p", t=UT)).then_inc(y_ready, 1)

            unit(0, first=True)
            unit(1)
            with dve.Fori(2, UNITS - 1) as i:
                unit(i)
            unit(UNITS - 1, last_unit=True)
            for i, m in TAIL:
                if (i, m) in SPLIT_BEFORE:
                    split_z_low(UNITS - 1, SPLIT_BEFORE.index((i, m)))
                if m < RELUS:
                    hidden_low(i, m)
                else:
                    write_y(i)

        @block.scalar
        def _(act):
            def split_high(n):
                table, c0, count = quarter(n)
                c0 += first_chunk[table]
                act.wait_ge(raw_landed[n % RAW], DMA * (n // RAW + 1))
                act.copy(high[:, c0:c0 + count, :], raw[n % RAW][:, 0:count, :]).then_inc(high_ready, 1)

            def copy_o(i, r, first):
                act.wait_ge(o_done, 2 * RP * i + 2 * r + 2)
                if not first:
                    act.wait_ge(g_done, NS * UT * i)
                for k in range(2):
                    last = act.copy(ET[:, :, :, ONEHOT[2 * r + k]],
                                    half(o_banks[r % 2][k], 0).rearrange("d (u p) -> d u p", u=UT))
                last.then_inc(o_copied, 1)

            def relu(i, m):
                act.wait_ge(m_done, RELUS * i + m + 1)
                wait_since(act, relu_low, RELUS * i + m - 1)
                h, n, b = (h1, m, b1_sb) if m < C1 else (h2, m - C1, b2_sb)
                act.activation(h[0][:, n, :], half(psO[m % 2], 0), ACT.Relu, bias=b[:, n:n + 1])
                act.activation(hidden[:, m % 2, :], half(psO[m % 2], 0), ACT.Relu, bias=b[:, n:n + 1])\
                   .then_inc(relu_done, 1)

            def split_weights_high(n):
                act.wait_ge(W_landed[n], DMA * (2 if n == 0 else 1))
                for raw_w, parts, shape in weight_parts[n]:
                    last = act.copy(shape(parts[0]), shape(raw_w))
                last.then_inc(W_high, 1)

            def split_z_high(i, u):
                act.wait_ge(z_landed[u], ZD * i + ZD)
                wait_since(act, m_done, RELUS * (i - 1) + C1)
                at = slice(u * P, (u + 1) * P)
                for cs, n in z_pieces:
                    last = act.copy(Zs[0][0:n, cs, at], Z[0:n, cs, at])
                last.then_inc(z_high, 1)

            split_high(0)
            split_high(1)
            for g in range(RG):
                act.wait_ge(rows_t_done, g + 1)
                act.copy(denseT[:, 4 * g:4 * g + 4, :], row_banks[g][QP:QP + ND, :, :]).then_inc(rows_t_act, 1)
            split_high(2)
            split_high(3)

            def unit(i, first=False, last_unit=False):
                for step, n in FIRST_A if first else LAST_A if last_unit else PHASE_A:
                    if step == "T" and n % 2:
                        copy_et(act, act.copy, i, 0, n, first, et_act)
                    elif step == "O" and first and n + 2 < 2 * RP:
                        split_high(2 * n + 4)
                        split_high(2 * n + 5)
                    elif step == "C":
                        copy_o(i, n, first)
                    elif step == "Z":
                        split_z_high(i - 1, n)
                    elif step == "G":
                        copy_gs(act, i - 1, 1, n)
                if first:
                    split_weights_high(0)
                for step, n in FIRST_B if first else LAST_B if last_unit else PHASE_B:
                    if step == "T" and n % 2:
                        copy_et(act, act.copy, i, 1, n, first, et_act)
                    elif step == "G":
                        copy_gs(act, i, 0, n)
                    elif step == "M" and n < RELUS:
                        relu(i - 1, n)

            unit(0, first=True)
            split_weights_high(1)
            split_weights_high(2)
            act.wait_ge(bias_landed, 2 * DMA)
            unit(1)
            with act.Fori(2, UNITS - 1) as i:
                unit(i)
            unit(UNITS - 1, last_unit=True)
            for s in range(NS):
                copy_gs(act, UNITS - 1, 1, s)
            for i, m in TAIL:
                if (i, m) in SPLIT_BEFORE:
                    split_z_high(UNITS - 1, SPLIT_BEFORE.index((i, m)))
                if m < RELUS:
                    relu(i, m)


def kernel(**inputs):
    import numpy as np
    import concourse.bacc as bacc
    from concourse.bass_utils import run_bass_kernel_spmd

    nc = bacc.Bacc("TRN2", target_bir_lowering=False, num_devices=1)
    arrays, aps = {}, {}
    for name, value in inputs.items():
        if name == "W_top1":
            value = np.asarray(value)[weight_order(inputs["ids"].shape[1], value.shape[0])]
        arrays[f"in_{name}"] = np.ascontiguousarray(value)
        a = arrays[f"in_{name}"]
        aps[name] = nc.dram_tensor(f"in_{name}", a.shape, mybir.dt.from_np(a.dtype), kind="ExternalInput").ap()
    batch, features = inputs["ids"].shape
    out = nc.dram_tensor("y_out", (batch, 1), F32, kind="ExternalOutput").ap()
    dlrm_tower(nc, aps["dense_ctx"], aps["ids"], [aps[f"tbl_{f}"] for f in range(features)],
               aps["W_top1"], aps["b_top1"], aps["W_top2"], aps["b_top2"], aps["W_top3"], out)
    result = run_bass_kernel_spmd(nc, [arrays], core_ids=[0])
    return result.results[0]["y_out"]
```
